# Optimizing a Trainium2 kernel written in Bass

```python
import numpy as np
import jax
import jax.numpy as jnp

def _softmax(x, axis=-1):
    return jax.nn.softmax(x, axis=axis)

def _gelu(x):
    return jax.nn.gelu(x, approximate=True)

def _silu(x):
    return jax.nn.silu(x)

def _sigmoid(x):
    return jax.nn.sigmoid(x)

def _layernorm(x, axis=-1, eps=1e-05):
    m = jnp.mean(x, axis=axis, keepdims=True)
    v = jnp.var(x, axis=axis, keepdims=True)
    return (x - m) / jnp.sqrt(v + eps)

def _scatter_add(tgt, idx, src, axis=0):
    return tgt.at[idx].add(src)

def _segment_sum(src, seg, n):
    return jax.ops.segment_sum(src, seg, n)
kernel_name = 'mk_macaron_d1_jaxref_r4_484ca6'

def setup_inputs(seed: int=0):
    np.random.seed(seed)
    _w = jnp.asarray

    def _L0_attn_setup():
        import jax, jax.numpy as jnp
        import numpy as np
        B, T, D = (4, 512, 256)
        H = 4
        K = D // H
        V = D // H
        M = 64
        GATE_LOGIT_NORMALIZER = 8.0
        NORM_EPS = 1e-05

        def _swish(x):
            return x * jax.nn.sigmoid(x)

        def _gsa_recurrence(q, k, v, s, g, scale):
            b, t, h, dk = q.shape
            dv = v.shape[-1]
            m = s.shape[-1]

            def step(carry, inp):
                hk, hv = carry
                q_t, k_t, v_t, s_t, g_t = inp
                ge = jnp.exp(g_t)
                hk = hk * ge[:, :, None, :] + k_t[..., :, None] * s_t[..., None, :]
                logits = jnp.einsum('bhk,bhkm->bhm', q_t * scale, hk)
                p = jax.nn.softmax(logits, axis=-1)
                hv = hv * ge[..., :, None] + s_t[..., :, None] * v_t[..., None, :]
                o_t = jnp.einsum('bhm,bhmv->bhv', p, hv)
                return ((hk, hv), o_t)
            init = (jnp.zeros((b, h, dk, m), q.dtype), jnp.zeros((b, h, m, dv), q.dtype))
            xs = tuple((jnp.moveaxis(a, 1, 0) for a in (q, k, v, s, g)))
            _, o = jax.lax.scan(step, init, xs)
            return jnp.moveaxis(o, 0, 1)
        key = jax.random.key(seed)
        ks = jax.random.split(key, 6)
        sc = lambda n: 1.0 / np.sqrt(n)
        return {'x': jax.random.normal(ks[0], (B, T, D), jnp.float32), 'Wq': jax.random.normal(ks[1], (D, H * K), jnp.float32) * sc(D), 'Wk': jax.random.normal(ks[2], (D, H * K), jnp.float32) * sc(D), 'Wv': jax.random.normal(ks[3], (D, H * V), jnp.float32) * sc(D), 'Wf': jax.random.normal(ks[4], (D, H * M), jnp.float32) * sc(D), 'g_norm_w': jnp.ones((V,), jnp.float32), 'Wo': jax.random.normal(ks[5], (H * V, D), jnp.float32) * sc(H * V)}
    _L0_attn_in = _L0_attn_setup()

    def _L0_ffn_setup():
        import jax, jax.numpy as jnp
        import numpy as np
        D_MODEL, D_FF, D2, DL = (256, 1024, 64, 64)
        D1 = D_FF // D2
        BATCH, SEQ = (2, 256)
        KERNEL_SCALE = D2 ** 0.5
        key = jax.random.key(seed)
        ks = jax.random.split(key, 7)
        xav = lambda k, shape, fan: jax.random.normal(k, shape, jnp.float32) * (2.0 / sum(fan)) ** 0.5
        x = jax.random.normal(ks[0], (BATCH, SEQ, D_MODEL), jnp.float32)
        m1 = xav(ks[1], (D_MODEL, DL), (D_MODEL, DL))
        m2 = xav(ks[2], (DL, D1, D2), (DL, D_FF))
        mb = jax.random.normal(ks[3], (D1, D2), jnp.float32)
        w1 = xav(ks[4], (D_MODEL, D1, D2), (D_MODEL, D_FF))
        w2 = xav(ks[5], (D2, D1, D_MODEL), (D_FF, D_MODEL)) * KERNEL_SCALE
        b2 = jax.random.normal(ks[6], (D_MODEL,), jnp.float32)
        return {'x': x, 'm1': m1, 'm2': m2, 'mb': mb, 'w1': w1, 'w2': w2, 'b2': b2}
    _L0_ffn_in = _L0_ffn_setup()
    _d = {'L0_attn_x': _L0_attn_in['x'], 'L0_attn_Wq': _L0_attn_in['Wq'], 'L0_attn_Wk': _L0_attn_in['Wk'], 'L0_attn_Wv': _L0_attn_in['Wv'], 'L0_attn_Wf': _L0_attn_in['Wf'], 'L0_attn_g_norm_w': _L0_attn_in['g_norm_w'], 'L0_attn_Wo': _L0_attn_in['Wo'], 'L0_ffn_m1': _L0_ffn_in['m1'], 'L0_ffn_m2': _L0_ffn_in['m2'], 'L0_ffn_mb': _L0_ffn_in['mb'], 'L0_ffn_w1': _L0_ffn_in['w1'], 'L0_ffn_w2': _L0_ffn_in['w2'], 'L0_ffn_b2': _L0_ffn_in['b2']}
    _x0 = _d['L0_attn_x']
    _d['L0_attn_x'] = jax.random.normal(jax.random.fold_in(jax.random.key(seed), 1), (32, 512, 256), dtype=_x0.dtype)
    del _x0
    return _d

def reference(L0_attn_x, L0_attn_Wq, L0_attn_Wk, L0_attn_Wv, L0_attn_Wf, L0_attn_g_norm_w, L0_attn_Wo, L0_ffn_m1, L0_ffn_m2, L0_ffn_mb, L0_ffn_w1, L0_ffn_w2, L0_ffn_b2):

    def _L0_attn_ref(x, Wq, Wk, Wv, Wf, g_norm_w, Wo):
        import jax, jax.numpy as jnp
        import numpy as np
        B, T, D = (4, 512, 256)
        H = 4
        K = D // H
        V = D // H
        M = 64
        GATE_LOGIT_NORMALIZER = 8.0
        NORM_EPS = 1e-05

        def _swish(x):
            return x * jax.nn.sigmoid(x)

        def _gsa_recurrence(q, k, v, s, g, scale):
            b, t, h, dk = q.shape
            dv = v.shape[-1]
            m = s.shape[-1]

            def step(carry, inp):
                hk, hv = carry
                q_t, k_t, v_t, s_t, g_t = inp
                ge = jnp.exp(g_t)
                hk = hk * ge[:, :, None, :] + k_t[..., :, None] * s_t[..., None, :]
                logits = jnp.einsum('bhk,bhkm->bhm', q_t * scale, hk)
                p = jax.nn.softmax(logits, axis=-1)
                hv = hv * ge[..., :, None] + s_t[..., :, None] * v_t[..., None, :]
                o_t = jnp.einsum('bhm,bhmv->bhv', p, hv)
                return ((hk, hv), o_t)
            init = (jnp.zeros((b, h, dk, m), q.dtype), jnp.zeros((b, h, m, dv), q.dtype))
            xs = tuple((jnp.moveaxis(a, 1, 0) for a in (q, k, v, s, g)))
            _, o = jax.lax.scan(step, init, xs)
            return jnp.moveaxis(o, 0, 1)
        b, t, d = x.shape
        q = _swish((x @ Wq).reshape(b, t, H, K))
        k = _swish((x @ Wk).reshape(b, t, H, K))
        v = (x @ Wv).reshape(b, t, H, V)
        f = jax.nn.log_sigmoid((x @ Wf).reshape(b, t, H, M)) / GATE_LOGIT_NORMALIZER
        s = 1.0 - jnp.exp(f)
        o = _gsa_recurrence(q, k, v, s, f, scale=K ** (-0.5))
        o = o * jax.lax.rsqrt(jnp.mean(o * o, axis=-1, keepdims=True) + NORM_EPS) * g_norm_w
        return o.reshape(b, t, H * V) @ Wo

    def _L0_ffn_ref(x, m1, m2, mb, w1, w2, b2):
        import jax, jax.numpy as jnp
        import numpy as np
        D_MODEL, D_FF, D2, DL = (256, 1024, 64, 64)
        D1 = D_FF // D2
        BATCH, SEQ = (2, 256)
        KERNEL_SCALE = D2 ** 0.5
        x_shape = x.shape
        xf = x.reshape(-1, x_shape[-1])
        d1 = w1.shape[1]
        lr = xf @ m1
        mask_logits = jnp.einsum('bl,lxy->bxy', lr, m2) + mb
        quant_mask = jnp.argmax(mask_logits, axis=-1)
        w1p = jnp.transpose(w1, (1, 2, 0))
        w2p = jnp.transpose(w2, (1, 0, 2))
        j = jnp.arange(d1)[None, :]
        w = w1p[j, quant_mask]
        mid = jnp.einsum('ai,aji->aj', xf, w)
        relu = jax.nn.relu(mid)
        v = w2p[j, quant_mask]
        res = jnp.einsum('ai,aij->aj', relu, v) + b2
        return res.reshape(x_shape)
    x = L0_attn_x
    x = x + 0.5 * _L0_ffn_ref(_layernorm(x, axis=-1), L0_ffn_m1, L0_ffn_m2, L0_ffn_mb, L0_ffn_w1, L0_ffn_w2, L0_ffn_b2)
    x = x + _L0_attn_ref(_layernorm(x, axis=-1), L0_attn_Wq, L0_attn_Wk, L0_attn_Wv, L0_attn_Wf, L0_attn_g_norm_w, L0_attn_Wo)
    x = x + 0.5 * _L0_ffn_ref(_layernorm(x, axis=-1), L0_ffn_m1, L0_ffn_m2, L0_ffn_mb, L0_ffn_w1, L0_ffn_w2, L0_ffn_b2)
    return x

_drawn_inputs = setup_inputs


def setup_inputs(seed=0):
    import zlib

    import numpy as np

    out = dict(_drawn_inputs(seed))
    spreads = {'L0_attn_g_norm_w': (1.0, 0.2)}
    factors = {'L0_attn_Wq': 8.0, 'L0_attn_Wk': 8.0}
    for name, (base, spread) in spreads.items():
        noise = np.random.default_rng([zlib.crc32(name.encode()), seed]).standard_normal(out[name].shape)
        drawn = base * np.exp(spread * noise) if base else spread * noise
        out[name] = jnp.asarray(drawn.astype(out[name].dtype))
    for name, factor in factors.items():
        out[name] = (out[name] * factor).astype(out[name].dtype)
    return out
```

```python
from contextlib import ExitStack

import concourse.bass as bass
from concourse import mybir

P = 128


class Tile:

    def __init__(self, n0, base, tiles, i=None, unroll=2):
        self.n = n0 if i is None else i * unroll + n0
        self.row = self.n - base
        self.slot = n0 % 2
        self.half = n0 // 2 if i is None else i * (unroll // 2) + n0 // 2
        self.ring = n0 % 4
        self.chunk = (n0 - base) % 4
        self.seq = (n0 - base) // 4 if i is None else i * (unroll // 4) + (n0 - base) // 4
        self.last = base + tiles

    def has(self, lag):
        return not isinstance(self.n, int) or 0 <= self.n - lag < self.last


def after(eng, sem, tile, lag=0):
    if tile.has(lag):
        eng.wait_ge(sem, tile.n + (1 - lag))


def after_dma(eng, sems, tile, lag=0):
    if tile.has(lag):
        eng.wait_ge(sems[tile.slot], tile.half * 16 + 16 * (1 - lag // 2))


def pipeline(eng, stages, tiles, base, unroll, longest_lag):
    low = min(o for _, o in stages)
    high = max(o for _, o in stages)

    def step(s, i=None):
        for stage, offset in stages:
            if i is not None or 0 <= s + offset < tiles:
                stage(Tile(base + s + offset, base, tiles, i, unroll))

    start = -(-(longest_lag - low) // unroll) * unroll
    trips = max((tiles - high - start) // unroll, 0)
    for s in range(-high, start):
        step(s)
    if trips:
        with eng.Fori(0, trips) as i:
            for s in range(unroll):
                step(start + s, i)
    for s in range(start + trips * unroll, tiles - low):
        step(s)


def build(nc, a, out, tiles, d_model, d_ff, d2, d_low, heads):
    f32, f16 = mybir.dt.float32, mybir.dt.float16
    ALU = mybir.AluOpType
    ACT = mybir.ActivationFunctionType
    AX = mybir.AxisListType

    KD = d_model // P
    KF = d_ff // P
    GROUPS = d_ff // d2
    BANK = 512
    EPS = 1e-5
    S_LOW = 64.0
    S_UP = 64.0
    S_DOWN = 16.0
    FFN_SCALE = 0.5 / (S_UP * S_DOWN)
    FLOOR = -3.0e38
    S_ATT = 64.0

    HD = d_model // heads
    PAIRS = d_model // P
    CHUNKS = 4
    GATE = 1.0 / 8.0
    QK_SCALE = float(HD) ** -0.5
    MIDDLE = P // 2

    ctx = ExitStack()
    with ctx:
        def sb(name, shape, dt=f32):
            return ctx.enter_context(nc.sbuf_tensor(name, shape, dt))

        def sem(name):
            return ctx.enter_context(nc.semaphore(name))

        def pair(name):
            return [sem(f"{name}0"), sem(f"{name}1")]

        def psum(scope, name, cols, dt=f32):
            return scope.enter_context(nc.psum_tensor(name, [P, cols], dt))

        ident16 = sb("ident16", [P, P], f16)
        w1_hl = sb("w1_hl", [P, 2, KD, d_ff], f16)
        w2_hl = sb("w2_hl", [P, 2, KF, d_model], f16)
        m1_hl = sb("m1_hl", [P, 2, KD, P], f16)
        m2_high2 = sb("m2_high2", [P, d_ff], f16)
        m2_low_mb = sb("m2_low_mb", [P, d_ff], f16)
        half_b2 = sb("half_b2", [P, d_model])
        restart = sb("restart", [P, d_ff])
        minus_half = sb("minus_half", [P, 1])
        eps_col = sb("eps_col", [P, 1])
        eps_sum_col = sb("eps_sum_col", [P, 1])

        ident32 = sb("ident32", [P, P])
        wqkfv_hl = sb("wqkfv_hl", [P, 2, KD, 4 * d_model], f16)
        wo_hl = sb("wo_hl", [P, 2, KD, d_model], f16)
        ramp16 = sb("ramp16", [P, P], f16)
        late16 = sb("late16", [P, P], f16)
        early16 = sb("early16", [P, P], f16)
        causal = sb("causal", [P, P])
        own_head = sb("own_head", [P, P])

        x_in = sb("x_in", [P, 2, d_model])
        x_res = sb("x_res", [P, 2, d_model])
        x_out = sb("x_out", [P, 2, d_model])
        stats = sb("stats", [P, 2, 6])
        moments = sb("moments", [P, 2, 2])
        var_eps = sb("var_eps", [P, 2, 1])
        rstd = sb("rstd", [P, 2, 1])
        xc = sb("xc", [P, 2, d_model])
        xn_hl = sb("xn_hl", [P, 2, 2, d_model], f16)
        xT_hl = sb("xT_hl", [P, 2, 2, KD, P], f16)
        step = sb("step", [P, 2, GROUPS, d2 + 2], f16)
        low_h1 = sb("low_h1", [P, 2, P], f16)

        names = ["w1", "w2", "m1", "m2", "mb"]
        loaded = {n: sem(f"loaded_{n}") for n in names + ["b2", "wqkfv", "wo", "g"]}
        mb_rows_placed = sem("mb_rows_placed")
        ident_zeroed, ident_made = sem("ident_zeroed"), sem("ident_made")
        consts_set = sem("consts_set")
        highs_made, lows_made = sem("highs_made"), sem("lows_made")
        mb_chain = sem("mb_chain")
        masks_zeroed, masks_made, wo_scaled = sem("masks_zeroed"), sem("masks_made"), sem("wo_scaled")

        with ExitStack() as staging:
            def st(name, shape, dt=f32):
                return staging.enter_context(nc.sbuf_tensor(name, shape, dt))

            w1_f = st("w1_f", [P, KD, d_ff])
            w2_f = st("w2_f", [P, KF, d_model])
            m1_f = st("m1_f", [P, KD, P])
            m2_f = st("m2_f", [P, d_ff])
            mb_f = st("mb_f", [1, d_ff])
            mb_rest = st("mb_rest", [1, 2, d_ff])
            mb_parts = st("mb_parts", [1, 3, d_ff], f16)
            b2_f = st("b2_f", [P, d_model])
            wqkfv_f = st("wqkfv_f", [P, KD, 4, d_model])
            wo_f = st("wo_f", [P, KD, d_model])
            g_f = st("g_f", [P, 1])
            tri_f = st("tri_f", [P, P])
            half_f = st("half_f", [P, P])

            with nc.Block() as block:
                @block.sync
                def _(sp):
                    sp.dma_start(m1_f[:, :, 0:d_low],
                                 a["m1"].rearrange("(k p) l -> p k l", p=P)).then_inc(loaded["m1"], 16)
                    sp.dma_start(m1_f[:, :, d_low:P],
                                 a["m1"].rearrange("(k p) l -> p k l", p=P)).then_inc(loaded["m1"], 16)
                    for h in range(2):
                        sp.dma_start(m2_f[h * d_low:(h + 1) * d_low, :],
                                     a["m2"].rearrange("l x y -> l (x y)")).then_inc(loaded["m2"], 16)
                    sp.dma_start(mb_f[:, :], a["mb"].rearrange("(a x) y -> a (x y)", a=1)).then_inc(loaded["mb"], 16)
                    sp.dma_start(w1_f[:, :, :],
                                 a["w1"].rearrange("(k p) x y -> p k (x y)", p=P)).then_inc(loaded["w1"], 16)
                    for h in range(2):
                        sp.dma_start(w2_f[h * d2:(h + 1) * d2, :, :],
                                     a["w2"].rearrange("y (c h) d -> h y c d", h=2)[h]).then_inc(loaded["w2"], 16)
                    sp.dma_start(b2_f[:, :], a["b2"].rearrange("(a d) -> a d", a=1).broadcast_to([P, d_model])
                                 ).then_inc(loaded["b2"], 16)
                    for n, w in enumerate(("Wq", "Wk", "Wf", "Wv")):
                        sp.dma_start(wqkfv_f[:, :, n], a[w].rearrange("(k p) d -> p k d", p=P)
                                     ).then_inc(loaded["wqkfv"], 16)
                    sp.dma_start(wo_f[:, :, :], a["Wo"].rearrange("(k p) d -> p k d", p=P)).then_inc(loaded["wo"], 16)
                    for h in range(P // HD):
                        sp.dma_start(g_f[h * HD:(h + 1) * HD, :], a["g"].rearrange("(v a) -> v a", a=1)
                                     ).then_inc(loaded["g"], 16)
                    sp.wait_ge(mb_chain, 5)
                    sp.wait_ge(consts_set, 1)
                    sp.dma_start(m2_low_mb[d_low:d_low + 3, :], mb_parts[0:1, :, :]).then_inc(mb_rows_placed, 16)
                    sp.wait_ge(mb_rows_placed, 16)

                @block.gpsimd
                def _(pool):
                    nc.gpsimd.memset(ident16[:, :], 0.0).then_inc(ident_zeroed, 1)
                    pool.wait_ge(ident_zeroed, 1)
                    nc.gpsimd.affine_select(out=ident16[:, :], in_=ident16[:, :], compare_op=ALU.not_equal,
                                            fill=1.0, base=0, pattern=[[-1, P]],
                                            channel_multiplier=1).then_inc(ident_made, 1)
                    nc.gpsimd.memset(minus_half[:, :], -0.5)
                    nc.gpsimd.memset(eps_col[:, :], EPS)
                    nc.gpsimd.memset(eps_sum_col[:, :], EPS * HD)
                    nc.gpsimd.memset(restart[:, :], 0.0).then_inc(ident_zeroed, 1)
                    pool.wait_ge(ident_zeroed, 2)
                    nc.gpsimd.memset(restart[:, 0:d_ff:d2], FLOOR).then_inc(ident_made, 1)

                    nc.gpsimd.memset(ident32[:, :], 0.0).then_inc(masks_zeroed, 1)
                    pool.wait_ge(masks_zeroed, 1)
                    nc.gpsimd.affine_select(out=ident32[:, :], in_=ident32[:, :], compare_op=ALU.not_equal,
                                            fill=1.0, base=0, pattern=[[-1, P]],
                                            channel_multiplier=1).then_inc(masks_made, 1)
                    nc.gpsimd.memset(causal[:, :], 1.0).then_inc(masks_zeroed, 1)
                    pool.wait_ge(masks_zeroed, 2)
                    nc.gpsimd.affine_select(out=causal[:, :], in_=causal[:, :], compare_op=ALU.is_ge,
                                            fill=0.0, base=0, pattern=[[1, P]],
                                            channel_multiplier=-1).then_inc(masks_made, 1)
                    nc.gpsimd.memset(half_f[:, :], 1.0).then_inc(masks_zeroed, 1)
                    pool.wait_ge(masks_zeroed, 3)
                    nc.gpsimd.affine_select(out=half_f[:, :], in_=half_f[:, :], compare_op=ALU.is_ge,
                                            fill=0.0, base=MIDDLE - 1, pattern=[[0, P]],
                                            channel_multiplier=-1).then_inc(masks_made, 1)
                    pool.wait_ge(masks_made, 3)
                    nc.gpsimd.tensor_scalar(early16[:, :], half_f[:, :], GATE, None, ALU.mult)
                    nc.gpsimd.tensor_scalar(late16[:, :], half_f[:, :], -GATE, GATE, ALU.mult, ALU.add)
                    nc.gpsimd.tensor_tensor(tri_f[:, :], causal[:, :], half_f[:, :],
                                            ALU.subtract).then_inc(masks_made, 1)
                    pool.wait_ge(masks_made, 4)
                    nc.gpsimd.tensor_scalar(ramp16[:, :], tri_f[:, :], GATE, None, ALU.mult)
                    nc.gpsimd.memset(own_head[:, :], 0.0).then_inc(masks_zeroed, 1)
                    pool.wait_ge(masks_zeroed, 4)
                    for h in range(P // HD):
                        nc.gpsimd.memset(own_head[h * HD:(h + 1) * HD, h * HD:(h + 1) * HD], 1.0
                                         ).then_inc(masks_made, 1)

                @block.scalar
                def _(act):
                    nc.scalar.preload_act_table_set("natural_log_exp_and_others")
                    act.wait_ge(loaded["m1"], 32)
                    nc.scalar.activation(m1_hl[:, 0], m1_f[:, :, :], ACT.Copy, scale=S_LOW).then_inc(highs_made, 1)
                    act.wait_ge(loaded["m2"], 32)
                    nc.scalar.activation(m2_high2[:, :], m2_f[:, :], ACT.Copy, scale=S_LOW).then_inc(highs_made, 1)
                    act.wait_ge(loaded["w1"], 16)
                    nc.scalar.activation(w1_hl[:, 0], w1_f[:, :, :], ACT.Copy, scale=S_UP).then_inc(highs_made, 1)
                    act.wait_ge(loaded["w2"], 32)
                    nc.scalar.activation(w2_hl[:, 0], w2_f[:, :, :], ACT.Copy, scale=S_DOWN).then_inc(highs_made, 1)
                    act.wait_ge(loaded["b2"], 16)
                    nc.scalar.activation(half_b2[:, :], b2_f[:, :], ACT.Copy, scale=0.5).then_inc(highs_made, 1)
                    act.wait_ge(loaded["wqkfv"], 64)
                    nc.scalar.activation(wqkfv_hl[:, 0], wqkfv_f[:, :, :, :].rearrange("p k n d -> p k (n d)"),
                                         ACT.Copy, scale=S_ATT).then_inc(highs_made, 1)
                    act.wait_ge(wo_scaled, 1)
                    nc.scalar.activation(wo_hl[:, 0], wo_f[:, :, :], ACT.Copy, scale=S_ATT).then_inc(highs_made, 1)

                @block.vector
                def _(dve):
                    nc.vector.memset(step[:, :, :, :], 0.0)
                    nc.vector.memset(m2_low_mb[d_low:P, :], 0.0).then_inc(consts_set, 1)
                    nc.vector.memset(low_h1[d_low:P, :, :], S_LOW)
                    dve.wait_ge(loaded["mb"], 16)
                    nc.vector.tensor_scalar(mb_parts[:, 0], mb_f[:, :], S_LOW, None, ALU.mult).then_inc(mb_chain, 1)
                    dve.wait_ge(mb_chain, 1)
                    nc.vector.scalar_tensor_tensor(mb_rest[:, 0], mb_f[:, :], S_LOW, mb_parts[:, 0],
                                                   ALU.mult, ALU.subtract).then_inc(mb_chain, 1)
                    dve.wait_ge(mb_chain, 2)
                    nc.vector.tensor_copy(mb_parts[:, 1], mb_rest[:, 0]).then_inc(mb_chain, 1)
                    dve.wait_ge(mb_chain, 3)
                    nc.vector.tensor_sub(mb_rest[:, 1], mb_rest[:, 0], mb_parts[:, 1]).then_inc(mb_chain, 1)
                    dve.wait_ge(mb_chain, 4)
                    nc.vector.tensor_copy(mb_parts[:, 2], mb_rest[:, 1]).then_inc(mb_chain, 1)
                    dve.wait_ge(highs_made, 1)
                    nc.vector.scalar_tensor_tensor(m1_hl[:, 1], m1_f[:, :, :], S_LOW, m1_hl[:, 0],
                                                   ALU.mult, ALU.subtract)
                    dve.wait_ge(highs_made, 2)
                    nc.vector.scalar_tensor_tensor(m2_low_mb[0:d_low, :], m2_f[0:d_low, :], S_LOW,
                                                   m2_high2[0:d_low, :], ALU.mult, ALU.subtract)
                    dve.wait_ge(highs_made, 3)
                    nc.vector.scalar_tensor_tensor(w1_hl[:, 1], w1_f[:, :, :], S_UP, w1_hl[:, 0],
                                                   ALU.mult, ALU.subtract)
                    dve.wait_ge(highs_made, 4)
                    nc.vector.scalar_tensor_tensor(w2_hl[:, 1], w2_f[:, :, :], S_DOWN, w2_hl[:, 0],
                                                   ALU.mult, ALU.subtract)
                    dve.wait_ge(highs_made, 6)
                    nc.vector.scalar_tensor_tensor(wqkfv_hl[:, 1],
                                                   wqkfv_f[:, :, :, :].rearrange("p k n d -> p k (n d)"), S_ATT,
                                                   wqkfv_hl[:, 0], ALU.mult, ALU.subtract)
                    dve.wait_ge(loaded["wo"], 16)
                    dve.wait_ge(loaded["g"], 32)
                    nc.vector.tensor_scalar(wo_f[:, :, :], wo_f[:, :, :], g_f[:, :], None,
                                            ALU.mult).then_inc(wo_scaled, 1)
                    dve.wait_ge(highs_made, 7)
                    nc.vector.scalar_tensor_tensor(wo_hl[:, 1], wo_f[:, :, :], S_ATT, wo_hl[:, 0],
                                                   ALU.mult, ALU.subtract)

        class Norm:

            def __init__(self, tag):
                self.loaded = pair(f"{tag}_x_loaded")
                self.stats_made, self.moments_made = sem(f"{tag}_stats_made"), sem(f"{tag}_moments_made")
                self.var_eps_made, self.rstd_made = sem(f"{tag}_var_eps_made"), sem(f"{tag}_rstd_made")
                self.centred = sem(f"{tag}_centred")
                self.high_made, self.low_made = sem(f"{tag}_xn_high_made"), sem(f"{tag}_xn_low_made")
                self.xT_done, self.xT_made = sem(f"{tag}_xT_done"), sem(f"{tag}_xT_made")

            def load(self, sp, t, src_t):
                after(sp, self.centred, t, lag=2)
                sp.dma_start(x_in[:, t.slot], src_t[t.row]).then_inc(self.loaded[t.slot], 16)

            def stats(self, dve, t):
                after(dve, self.centred, t, lag=2)
                after(dve, self.var_eps_made, t, lag=2)
                after_dma(dve, self.loaded, t)
                nc.vector.bn_stats(stats[:, t.slot], x_in[:, t.slot]).then_inc(self.stats_made, 1)

            def aggregate(self, dve, t):
                if isinstance(t.n, int):
                    after(dve, self.stats_made, t)
                nc.vector.bn_aggr(moments[:, t.slot], stats[:, t.slot]).then_inc(self.moments_made, 1)

            def centre(self, pool, t):
                after(pool, self.moments_made, t)
                nc.gpsimd.tensor_tensor(var_eps[:, t.slot], moments[:, t.slot, 1:2], eps_col[:, 0:1],
                                        ALU.add).then_inc(self.var_eps_made, 1)
                after(pool, self.var_eps_made, t)
                after(pool, self.low_made, t, lag=2)
                nc.gpsimd.tensor_tensor(rstd[:, t.slot], var_eps[:, t.slot], minus_half[:, 0:1],
                                        ALU.pow).then_inc(self.rstd_made, 1)
                nc.gpsimd.tensor_tensor(xc[:, t.slot], x_in[:, t.slot],
                                        moments[:, t.slot, 0:1].broadcast_to([P, d_model]), ALU.subtract).then_inc(self.centred, 1)

            def high(self, act, t):
                after(act, self.rstd_made, t)
                after(act, self.centred, t)
                after(act, self.xT_done, t, lag=2)
                nc.scalar.activation(xn_hl[:, t.slot, 0], xc[:, t.slot], ACT.Copy,
                                     scale=rstd[:, t.slot]).then_inc(self.high_made, 1)

            def low(self, dve, t):
                after(dve, self.high_made, t)
                nc.vector.scalar_tensor_tensor(xn_hl[:, t.slot, 1], xc[:, t.slot], rstd[:, t.slot],
                                               xn_hl[:, t.slot, 0], ALU.mult,
                                               ALU.subtract).then_inc(self.low_made, 1)

            def transpose(self, pe, t, xT_ps):
                after(pe, self.low_made, t)
                after(pe, self.xT_made, t, lag=1)
                for part in range(2):
                    for k in range(KD):
                        at = (part * KD + k) * P
                        last = nc.tensor.transpose(xT_ps[:, at:at + P],
                                                   xn_hl[:, t.slot, part, k * P:(k + 1) * P], ident16[:, :])
                last.then_inc(self.xT_done, 1)

            def evacuate(self, act, t, xT_ps):
                after(act, self.xT_done, t)
                nc.scalar.activation(xT_hl[:, t.slot], xT_ps, ACT.Copy).then_inc(self.xT_made, 1)

        def three(dst, left, right, blocks):
            last = None
            for k in range(blocks):
                for lp, rp in ((0, 0), (0, 1), (1, 0)):
                    last = nc.tensor.matmul(dst, left(lp, k), right(rp, k), start=(k == 0 and lp == rp),
                                            stop=(k == blocks - 1 and lp == 1))
            return last

        def ffn_phase(src, dst, base):
            src_t = src.rearrange("(t p) d -> t p d", p=P)
            dst_t = dst.rearrange("(t p) d -> t p d", p=P)
            UNROLL, LONGEST_LAG = 8, 2

            scope = ExitStack()

            def fb(name, shape, dt=f32):
                return scope.enter_context(nc.sbuf_tensor(f"{name}_{base}", shape, dt))

            logits_ps = psum(scope, f"logits_ps_{base}", 2 * BANK)
            mid_ps = psum(scope, f"mid_ps_{base}", 2 * BANK)
            hotT_ps = psum(scope, f"hotT_ps_{base}", 2 * BANK, f16)
            front_ps = psum(scope, f"front_ps_{base}", BANK)
            res_ps = psum(scope, f"res_ps_{base}", BANK)
            xT_ps = front_ps[:, 0:BANK // 2].bitcast(f16)
            low_ps = front_ps[:, BANK // 2:BANK // 2 + P]

            low_hl = fb("low_hl", [P, 2, P], f16)
            runmax = fb("runmax", [P, d_ff])
            onehot = fb("onehot", [P, 2, d_ff], f16)
            hotT = fb("hotT", [P, 2, KF, P], f16)
            midT_hl = fb("midT_hl", [P, 2, 2, KF, P], f16)

            with nc.Block() as block:
                @block.sync
                def _(sp):
                    def load_residual(t):
                        after(sp, out_made, t, lag=2)
                        sp.dma_start(x_res[:, t.slot], src_t[t.row]).then_inc(res_loaded[t.slot], 16)

                    def store(t):
                        after(sp, out_made, t)
                        sp.dma_start(dst_t[t.row], x_out[:, t.slot]).then_inc(out_stored[t.slot], 16)

                    pipeline(sp, [(lambda t: norm.load(sp, t, src_t), 4), (load_residual, 0), (store, -1)], tiles, base, UNROLL, LONGEST_LAG)
                    for s in range(2):
                        sp.wait_ge(out_stored[s], 16 * (base + tiles) // 2)

                @block.gpsimd
                def _(pool):
                    def add_bias(t):
                        after_dma(pool, res_loaded, t)
                        nc.gpsimd.tensor_tensor(x_res[:, t.slot], x_res[:, t.slot], half_b2[:, :],
                                                ALU.add).then_inc(res_biased, 1)

                    pipeline(pool, [(lambda t: norm.centre(pool, t), 3), (add_bias, -1)],
                             tiles, base, UNROLL, LONGEST_LAG)

                @block.scalar
                def _(act):
                    def evacuate_hot(t):
                        after(act, hotT_done, t)
                        after(act, masked, t, lag=2)
                        nc.scalar.activation(hotT[:, t.slot], hotT_ps[:, :], ACT.Copy).then_inc(hotT_made, 1)

                    def mid_high(t):
                        after(act, mid_done, t)
                        after(act, res_done, t, lag=2)
                        nc.scalar.activation(midT_hl[:, t.slot, 0], mid_ps[:, :], ACT.Relu).then_inc(mid_high_made, 1)

                    def low_high(t):
                        after(act, low_done, t)
                        after(act, logits_done, t, lag=2)
                        nc.scalar.activation(low_hl[:, t.slot], low_ps, ACT.Copy).then_inc(low_high_made, 1)
                        nc.scalar.activation(low_h1[0:d_low, t.slot], low_ps[0:d_low, :],
                                             ACT.Copy).then_inc(low_h1_made, 1)

                    def evacuate_xT(t):
                        after(act, mid_done, t, lag=2)
                        norm.evacuate(act, t, xT_ps)

                    pipeline(act, [(mid_high, 0), (low_high, 1), (lambda t: norm.high(act, t), 3),
                                   (evacuate_hot, 0), (evacuate_xT, 2)],
                             tiles, base, UNROLL, LONGEST_LAG)

                @block.vector
                def _(dve):
                    def first_max(t):
                        after(dve, logits_done, t)
                        nc.vector.tensor_tensor_scan(runmax[:, :], restart[:, :], logits_ps[:, :], FLOOR,
                                                     ALU.add, ALU.max).then_inc(runmax_made, 1)
                        after(dve, runmax_made, t)
                        groups = runmax[:, :].rearrange("p (g d) -> p g d", g=GROUPS)
                        nc.vector.tensor_tensor(step[:, t.slot, :, 1:d2 + 1], groups,
                                                groups[:, :, d2 - 1:d2].broadcast_to([P, GROUPS, d2]),
                                                ALU.is_equal).then_inc(step_made, 1)

                    def pick(t):
                        after(dve, step_made, t)
                        after(dve, hotT_done, t, lag=2)
                        nc.vector.tensor_tensor(
                            onehot[:, t.slot].rearrange("p (g d) -> p g d", g=GROUPS),
                            step[:, t.slot, :, 1:d2 + 1], step[:, t.slot, :, 0:d2],
                            ALU.subtract).then_inc(onehot_made, 1)

                    def mid_low(t):
                        after(dve, mid_high_made, t)
                        nc.vector.scalar_tensor_tensor(midT_hl[:, t.slot, 1], mid_ps[:, :], 0.0,
                                                       midT_hl[:, t.slot, 0], ALU.max,
                                                       ALU.subtract).then_inc(mid_low_made, 1)

                    def low_low(t):
                        after(dve, low_high_made, t)
                        nc.vector.tensor_tensor(low_hl[d_low:P, t.slot], low_ps[d_low:P, :],
                                                low_hl[d_low:P, t.slot], ALU.subtract).then_inc(low_low_made, 1)

                    def mask(t):
                        after(dve, mid_low_made, t)
                        after(dve, hotT_made, t)
                        nc.vector.tensor_tensor(midT_hl[:, t.slot], midT_hl[:, t.slot],
                                                hotT[:, t.slot:t.slot + 1].broadcast_to([P, 2, KF, P]),
                                                ALU.mult).then_inc(masked, 1)

                    def finish(t):
                        after(dve, res_done, t)
                        after(dve, res_biased, t)
                        after_dma(dve, out_stored, t, lag=2)
                        nc.vector.scalar_tensor_tensor(x_out[:, t.slot],
                                                       res_ps[:, 0:d_model], FFN_SCALE,
                                                       x_res[:, t.slot], ALU.mult, ALU.add).then_inc(out_made, 1)

                    pipeline(dve, [(lambda t: norm.stats(dve, t), 3), (mask, -1), (first_max, 0),
                                   (lambda t: norm.aggregate(dve, t), 3), (pick, 0), (low_low, 1), (mid_low, 0),
                                   (finish, -1), (lambda t: norm.low(dve, t), 3)],
                             tiles, base, UNROLL, LONGEST_LAG)

                @block.tensor
                def _(pe):
                    def mask_logits(t):
                        after(pe, low_low_made, t)
                        after(pe, low_h1_made, t)
                        after(pe, runmax_made, t, lag=1)
                        for c in range(2):
                            cols = slice(c * BANK, (c + 1) * BANK)
                            nc.tensor.matmul(logits_ps[:, cols], low_hl[:, t.slot], m2_high2[:, cols],
                                             start=True, stop=False)
                            last = nc.tensor.matmul(logits_ps[:, cols], low_h1[:, t.slot], m2_low_mb[:, cols],
                                                    start=False, stop=True)
                        last.then_inc(logits_done, 1)

                    def transpose_hot(t):
                        after(pe, onehot_made, t)
                        after(pe, hotT_made, t, lag=1)
                        for c in range(KF):
                            last = nc.tensor.transpose(hotT_ps[:, c * P:(c + 1) * P],
                                                       onehot[:, t.slot, c * P:(c + 1) * P], ident16[:, :])
                        last.then_inc(hotT_done, 1)

                    def up(t):
                        after(pe, mid_high_made, t, lag=1)
                        after(pe, mid_low_made, t, lag=1)
                        for c in range(KF):
                            cols = slice(c * P, (c + 1) * P)
                            last = three(mid_ps[:, cols], lambda p, k: w1_hl[:, p, k, cols],
                                         lambda p, k: xT_hl[:, t.slot, p, k], KD)
                        last.then_inc(mid_done, 1)

                    def low_rank(t):
                        after(pe, norm.xT_made, t)
                        after(pe, low_low_made, t, lag=1)
                        after(pe, low_h1_made, t, lag=1)
                        three(low_ps, lambda p, k: m1_hl[:, p, k], lambda p, k: xT_hl[:, t.slot, p, k],
                              KD).then_inc(low_done, 1)

                    def down(t):
                        after(pe, masked, t)
                        after(pe, out_made, t, lag=1)
                        three(res_ps[:, 0:d_model],
                              lambda p, k: midT_hl[:, t.slot, p, k], lambda p, k: w2_hl[:, p, k],
                              KF).then_inc(res_done, 1)

                    def transpose_x(t):
                        after(pe, low_h1_made, t, lag=1)
                        after(pe, low_low_made, t, lag=1)
                        norm.transpose(pe, t, xT_ps)

                    pipeline(pe, [(mask_logits, 0), (up, 0), (low_rank, 1), (down, -1), (transpose_hot, 0),
                                  (transpose_x, 2)],
                             tiles, base, UNROLL, LONGEST_LAG)
            scope.close()

        def attention_phase(src, dst):
            src_t = src.rearrange("(t p) d -> t p d", p=P)
            dst_t = dst.rearrange("(t p) d -> t p d", p=P)
            base, UNROLL, LONGEST_LAG = 0, 4, 4
            D = d_model

            scope = ExitStack()

            def fb(name, shape, dt=f32):
                return scope.enter_context(nc.sbuf_tensor(name, shape, dt))

            bank_qk = psum(scope, "bank_qk", BANK)
            bank_fv = psum(scope, "bank_fv", BANK)
            bank_16 = psum(scope, "bank_16", BANK)
            bank_qkT = psum(scope, "bank_qkT", BANK)
            bank_pair = psum(scope, "bank_pair", 2 * BANK)
            bank_rows = psum(scope, "bank_rows", BANK)
            bank_sT = psum(scope, "bank_sT", BANK)
            xT_ps = bank_16[:, 0:BANK].bitcast(f16)[:, 0:2 * D]
            by_pair = bank_pair[:, :].rearrange("p (z c) -> p z c", z=2)[:, :, 0:PAIRS * P]
            by_pair4 = by_pair.rearrange("p z (a t) -> p z a t", a=PAIRS)

            qkfv = fb("qkfv", [P, 4, 4, D])
            absneg = fb("absneg", [P, 2, 3, D])
            lnone = fb("lnone", [P, 2, 3, D])
            logsig = fb("logsig", [P, 2, 3, D])
            gate_hl = fb("gate_hl", [P, 2, 2, D], f16)
            keep = fb("keep", [P, 2, D])
            sig = fb("sig", [P, 2, 2, D])
            qk = fb("qk", [P, 4, 2, D])
            qkT = fb("qkT", [P, 2, 2 * PAIRS, P])
            expG = fb("expG", [P, 4, D])
            expnG = fb("expnG", [P, 2, D])
            decay_rows = fb("decay_rows", [P, 2, D])
            decay_own = fb("decay_own", [P, 2, D])
            decay_col = fb("decay_col", [P, 2, PAIRS])
            St = fb("St", [P, 4, D])
            StT = fb("StT", [P, 2, PAIRS, P])
            PtT = fb("PtT", [P, 2, PAIRS, P])
            A_masked = fb("A_masked", [P, 2, PAIRS, P])
            B_masked = fb("B_masked", [P, 2, PAIRS, P])
            logit = fb("logit", [P, 2, D])
            centred_logit = fb("centred_logit", [P, 2, D])
            top = fb("top", [P, 2, heads])
            prob = fb("prob", [P, 2, D])
            total = fb("total", [P, 2, heads])
            inv_total = fb("inv_total", [P, 2, heads])
            Pt = fb("Pt", [P, 2, D])
            Hk = fb("Hk", [P, PAIRS, P])
            Hk_sum = fb("Hk_sum", [P, PAIRS, P])
            Hv = fb("Hv", [P, PAIRS, P])
            Hv_sum = fb("Hv_sum", [P, PAIRS, P])
            o_raw = fb("o_raw", [P, 2, D])
            o_sq = fb("o_sq", [P, 2, D])
            o_sum = fb("o_sum", [P, 2, heads])
            o_sum_eps = fb("o_sum_eps", [P, 2, heads])
            o_rms = fb("o_rms", [P, 2, heads])
            o_norm = fb("o_norm", [P, 2, D])
            o_hl = fb("o_hl", [P, 2, 2, D], f16)
            oT = fb("oT", [P, 2, 2, KD, P], f16)

            norm = Norm("att")
            res_loaded, out_stored = pair("att_res_loaded"), pair("att_out_stored")
            S = {n: sem(n) for n in (
                "fv_done", "gates_made", "qk_done", "qk_raw_made",
                "gate_abs", "gate_exp", "gate_ln", "gate_logsig", "gate_high", "gate_low", "keep_made",
                "qk_abs", "qk_exp", "qk_ln", "qk_logsig", "sig_made", "qk_made",
                "G_done", "expG_made", "expnG_made", "decay_rows_made", "decay_own_made",
                "decay_col_done", "decay_col_made", "St_made",
                "qkT_done", "qkT_made", "A_done", "A_made", "StT_done", "StT_made",
                "L_done", "logit_made", "top_made", "logit_centred", "prob_made", "total_made",
                "inv_total_made", "Pt_made", "PtT_done", "PtT_made", "B_done", "B_made",
                "Hk_update_done", "Hk_sum_made", "Hk_made", "Hv_update_done", "Hv_sum_made", "Hv_made",
                "o_done", "o_raw_made", "o_sq_made", "o_sum_made", "o_sum_eps_made", "o_rms_made",
                "o_norm_made", "o_high_made", "o_low_made", "oT_done", "oT_made",
                "proj_done", "att_res_added")}

            def heads_of(ap):
                return ap.rearrange("p (h m) -> p h m", h=heads)

            def pairs_of(ap):
                return ap.rearrange("p (a c) -> p a c", a=PAIRS)

            def per_head(ap):
                return ap.rearrange("p (h a) -> p h a", a=1).broadcast_to([P, heads, HD])

            def after_chunk(eng, sem, t, counted, lag=0):
                chunk = (t.chunk - lag) % CHUNKS
                if chunk in counted and t.has(lag):
                    seq = t.seq + (t.chunk - lag) // CHUNKS
                    eng.wait_ge(sem, seq * len(counted) + chunk - counted[0] + 1)

            LATER = range(1, CHUNKS)
            EARLIER = range(0, CHUNKS - 1)

            with nc.Block() as block:
                @block.sync
                def _(sp):
                    def load_residual(t):
                        after(sp, S["att_res_added"], t, lag=2)
                        sp.dma_start(x_res[:, t.slot], src_t[t.row]).then_inc(res_loaded[t.slot], 16)

                    def store(t):
                        after(sp, S["att_res_added"], t)
                        sp.dma_start(dst_t[t.row], x_out[:, t.slot]).then_inc(out_stored[t.slot], 16)

                    pipeline(sp, [(lambda t: norm.load(sp, t, src_t), 4), (store, -2), (load_residual, -1)],
                             tiles, base, UNROLL, LONGEST_LAG)
                    for s in range(2):
                        sp.wait_ge(out_stored[s], 16 * tiles // 2)

                @block.gpsimd
                def _(pool):
                    def gate_low(t):
                        after(pool, S["gate_high"], t)
                        nc.gpsimd.tensor_tensor(gate_hl[:, t.slot, 1], logsig[:, t.slot, 2], gate_hl[:, t.slot, 0],
                                                ALU.subtract).then_inc(S["gate_low"], 1)

                    def swish(t):
                        after(pool, S["sig_made"], t)
                        after(pool, S["o_done"], t, lag=4)
                        nc.gpsimd.tensor_tensor(qk[:, t.ring], qkfv[:, t.ring, 0:2], sig[:, t.slot],
                                                ALU.mult).then_inc(S["qk_made"], 1)

                    def own_decay(t):
                        if t.chunk:
                            after_chunk(pool, S["decay_rows_made"], t, LATER)
                            after(pool, S["L_done"], t, lag=2)
                            nc.gpsimd.tensor_tensor(
                                pairs_of(decay_own[:, t.slot]), pairs_of(decay_rows[:, t.slot]),
                                own_head[:, :].rearrange("p (a c) -> p a c", a=1).broadcast_to([P, PAIRS, P]),
                                ALU.mult).then_inc(S["decay_own_made"], 1)

                    def weight(t):
                        after(pool, S["prob_made"], t)
                        after(pool, S["PtT_done"], t, lag=2)
                        nc.gpsimd.tensor_tensor(Pt[:, t.slot], prob[:, t.slot], expG[:, t.ring],
                                                ALU.mult).then_inc(S["Pt_made"], 1)

                    def rms(t):
                        after(pool, S["o_sum_made"], t)
                        nc.gpsimd.tensor_tensor(o_sum_eps[:, t.slot], o_sum[:, t.slot],
                                                eps_sum_col[:, :].broadcast_to([P, heads]),
                                                ALU.add).then_inc(S["o_sum_eps_made"], 1)
                        after(pool, S["o_sum_eps_made"], t)
                        nc.gpsimd.tensor_tensor(o_rms[:, t.slot], o_sum_eps[:, t.slot],
                                                minus_half[:, :].broadcast_to([P, heads]),
                                                ALU.pow).then_inc(S["o_rms_made"], 1)
                        after(pool, S["o_rms_made"], t)
                        after(pool, S["o_low_made"], t, lag=2)
                        nc.gpsimd.tensor_tensor(heads_of(o_norm[:, t.slot]), heads_of(o_raw[:, t.slot]),
                                                per_head(o_rms[:, t.slot]), ALU.mult).then_inc(S["o_norm_made"], 1)

                    pipeline(pool, [(rms, -2), (gate_low, 1), (lambda t: norm.centre(pool, t), 3), (swish, 1),
                                    (weight, 0), (own_decay, 1)],
                             tiles, base, UNROLL, LONGEST_LAG)

                @block.scalar
                def _(act):
                    def evacuate_PtT(t):
                        after(act, S["PtT_done"], t)
                        after(act, S["o_done"], t, lag=2)
                        nc.scalar.activation(PtT[:, t.slot], pairs_of(bank_sT[:, 0:D]), ACT.Copy
                                             ).then_inc(S["PtT_made"], 1)

                    def evacuate_fv(t):
                        after(act, S["fv_done"], t)
                        after(act, S["o_done"], t, lag=4)
                        nc.scalar.activation(qkfv[:, t.ring, 2:4], bank_fv[:, :].rearrange("p (n d) -> p n d", n=2),
                                             ACT.Copy, scale=1.0 / S_ATT).then_inc(S["gates_made"], 1)

                    def gate_softplus(t):
                        after(act, S["gate_abs"], t)
                        nc.scalar.activation(absneg[:, t.slot, 2], absneg[:, t.slot, 2], ACT.Exp
                                             ).then_inc(S["gate_exp"], 1)
                        after(act, S["gate_exp"], t)
                        nc.scalar.activation(lnone[:, t.slot, 2], absneg[:, t.slot, 2], ACT.Ln, bias=1.0
                                             ).then_inc(S["gate_ln"], 1)

                    def evacuate_qkT(t):
                        after(act, S["qkT_done"], t)
                        nc.scalar.activation(qkT[:, t.slot], bank_qkT[:, :].rearrange("p (a t) -> p a t", t=P),
                                             ACT.Copy).then_inc(S["qkT_made"], 1)

                    def evacuate_qk(t):
                        after(act, S["qk_done"], t)
                        nc.scalar.activation(qkfv[:, t.ring, 0:2], bank_qk[:, :].rearrange("p (n d) -> p n d", n=2),
                                             ACT.Copy, scale=1.0 / S_ATT).then_inc(S["qk_raw_made"], 1)

                    def gate_high(t):
                        after(act, S["gate_logsig"], t)
                        after(act, S["G_done"], t, lag=1)
                        after_chunk(act, S["decay_col_done"], t, LATER, lag=1)
                        nc.scalar.activation(gate_hl[:, t.slot, 0], logsig[:, t.slot, 2], ACT.Copy
                                             ).then_inc(S["gate_high"], 1)
                        after(act, S["St_made"], t, lag=2)
                        nc.scalar.activation(keep[:, t.slot], logsig[:, t.slot, 2], ACT.Exp, scale=GATE
                                             ).then_inc(S["keep_made"], 1)

                    def qk_softplus(t):
                        after(act, S["qk_abs"], t)
                        nc.scalar.activation(absneg[:, t.slot, 0:2], absneg[:, t.slot, 0:2], ACT.Exp
                                             ).then_inc(S["qk_exp"], 1)
                        after(act, S["qk_exp"], t)
                        nc.scalar.activation(lnone[:, t.slot, 0:2], absneg[:, t.slot, 0:2], ACT.Ln, bias=1.0
                                             ).then_inc(S["qk_ln"], 1)

                    def evacuate_StT(t):
                        after(act, S["StT_done"], t)
                        after(act, S["B_done"], t, lag=2)
                        nc.scalar.activation(StT[:, t.slot], pairs_of(bank_sT[:, 0:D]), ACT.Copy
                                             ).then_inc(S["StT_made"], 1)

                    def square(t):
                        after(act, S["o_raw_made"], t)
                        after(act, S["o_sum_made"], t, lag=2)
                        nc.scalar.activation(o_sq[:, t.slot], o_raw[:, t.slot], ACT.Square
                                             ).then_inc(S["o_sq_made"], 1)

                    def sigmoid(t):
                        after(act, S["qk_logsig"], t)
                        after(act, S["qk_made"], t, lag=2)
                        nc.scalar.activation(sig[:, t.slot], logsig[:, t.slot, 0:2], ACT.Exp
                                             ).then_inc(S["sig_made"], 1)

                    def o_high(t):
                        after(act, S["o_norm_made"], t)
                        after(act, S["oT_done"], t, lag=2)
                        nc.scalar.activation(o_hl[:, t.slot, 0], o_norm[:, t.slot], ACT.Copy
                                             ).then_inc(S["o_high_made"], 1)

                    def softmax_exp(t):
                        after(act, S["logit_centred"], t)
                        after(act, S["Pt_made"], t, lag=2)
                        after(act, S["total_made"], t, lag=2)
                        nc.scalar.activation(prob[:, t.slot], centred_logit[:, t.slot], ACT.Exp, scale=QK_SCALE
                                             ).then_inc(S["prob_made"], 1)

                    def exp_sums(t):
                        after(act, S["G_done"], t)
                        after(act, S["Pt_made"], t, lag=4)
                        nc.scalar.activation(expnG[:, t.slot], bank_fv[:, 0:D], ACT.Exp, scale=-1.0
                                             ).then_inc(S["expnG_made"], 1)
                        nc.scalar.activation(expG[:, t.ring], bank_fv[:, 0:D], ACT.Exp).then_inc(S["expG_made"], 1)
                        if t.chunk:
                            nc.scalar.activation(decay_rows[:, t.slot], bank_fv[:, D:2 * D], ACT.Exp
                                                 ).then_inc(S["decay_rows_made"], 1)

                    def evacuate_oT(t):
                        after(act, S["oT_done"], t)
                        after(act, S["proj_done"], t, lag=2)
                        nc.scalar.activation(oT[:, t.slot], xT_ps, ACT.Copy).then_inc(S["oT_made"], 1)

                    def exp_decay_col(t):
                        if t.chunk:
                            after_chunk(act, S["decay_col_done"], t, LATER)
                            after_chunk(act, S["Hv_made"], t, LATER, lag=2)
                            nc.scalar.activation(decay_col[:, t.slot], bank_16[:, 0:PAIRS], ACT.Exp
                                                 ).then_inc(S["decay_col_made"], 1)

                    def evacuate_xT(t):
                        after(act, S["qk_done"], t, lag=2)
                        norm.evacuate(act, t, xT_ps)

                    pipeline(act, [(evacuate_qkT, 0), (evacuate_fv, 1), (gate_softplus, 1), (o_high, -2),
                                   (evacuate_qk, 1), (evacuate_StT, 0), (gate_high, 1), (evacuate_oT, -2),
                                   (evacuate_PtT, -1), (qk_softplus, 1), (softmax_exp, 0), (exp_decay_col, 1),
                                   (sigmoid, 1), (evacuate_xT, 2), (exp_sums, 1), (lambda t: norm.high(act, t), 3),
                                   (square, -1)],
                             tiles, base, UNROLL, LONGEST_LAG)

                @block.vector
                def _(dve):
                    def negated_abs(t, which, made):
                        x = qkfv[:, t.ring, which]
                        nc.vector.scalar_tensor_tensor(absneg[:, t.slot, which], x, -1.0, x, ALU.mult,
                                                       ALU.min).then_inc(made, 1)

                    def log_sigmoid(t, which, made):
                        nc.vector.scalar_tensor_tensor(logsig[:, t.slot, which], qkfv[:, t.ring, which], 0.0,
                                                       lnone[:, t.slot, which], ALU.min,
                                                       ALU.subtract).then_inc(made, 1)

                    def gate_abs(t):
                        after(dve, S["gates_made"], t)
                        after(dve, S["gate_ln"], t, lag=2)
                        negated_abs(t, 2, S["gate_abs"])

                    def gate_logsig(t):
                        after(dve, S["gate_ln"], t)
                        after(dve, S["gate_low"], t, lag=2)
                        after(dve, S["keep_made"], t, lag=2)
                        log_sigmoid(t, 2, S["gate_logsig"])

                    def qk_abs(t):
                        after(dve, S["qk_raw_made"], t)
                        after(dve, S["qk_ln"], t, lag=2)
                        negated_abs(t, slice(0, 2), S["qk_abs"])

                    def qk_logsig(t):
                        after(dve, S["qk_ln"], t)
                        after(dve, S["sig_made"], t, lag=2)
                        log_sigmoid(t, slice(0, 2), S["qk_logsig"])

                    def mask_heads(dst, t, done, made):
                        after(dve, done, t)
                        nc.vector.tensor_tensor(
                            dst[:, :, :, :], by_pair4,
                            causal[:, :].rearrange("p (z a t) -> p z a t", z=1, a=1).broadcast_to([P, 2, PAIRS, P]),
                            ALU.mult).then_inc(made, 1)

                    def mask_B(t):
                        after(dve, S["o_done"], t, lag=1)
                        mask_heads(B_masked, t, S["B_done"], S["B_made"])

                    def mask_A(t):
                        after(dve, S["L_done"], t, lag=1)
                        mask_heads(A_masked, t, S["A_done"], S["A_made"])

                    def divide_o(t):
                        after(dve, S["o_done"], t)
                        after(dve, S["inv_total_made"], t)
                        after(dve, S["o_norm_made"], t, lag=2)
                        nc.vector.tensor_tensor(heads_of(o_raw[:, t.slot]), heads_of(bank_rows[:, 0:D]),
                                                per_head(inv_total[:, t.slot]), ALU.mult
                                                ).then_inc(S["o_raw_made"], 1)

                    def sum_squares(t):
                        after(dve, S["o_sq_made"], t)
                        nc.vector.tensor_reduce(o_sum[:, t.slot], heads_of(o_sq[:, t.slot]), AX.X, ALU.add
                                                ).then_inc(S["o_sum_made"], 1)

                    def add_Hv(t):
                        if t.chunk == CHUNKS - 1:
                            return
                        after_chunk(dve, S["Hv_update_done"], t, EARLIER)
                        update = pairs_of(bank_qkT[:, 0:D])
                        if t.chunk:
                            nc.vector.tensor_tensor(Hv_sum[:, :, :], Hv[:, :, :], update, ALU.add
                                                    ).then_inc(S["Hv_sum_made"], 1)
                        else:
                            nc.vector.tensor_copy(Hv_sum[:, :, :], update).then_inc(S["Hv_sum_made"], 1)

                    def decay_Hv(t):
                        if t.chunk == CHUNKS - 1:
                            return
                        after_chunk(dve, S["Hv_sum_made"], t, EARLIER)
                        after_chunk(dve, S["decay_col_made"], t, LATER, lag=-1)
                        after(dve, S["o_done"], t)
                        for a in range(PAIRS):
                            last = nc.vector.scalar_tensor_tensor(
                                Hv[:, a], Hv_sum[:, a], decay_col[:, 1 - t.slot, a:a + 1], own_head[:, :],
                                ALU.mult, ALU.mult)
                        last.then_inc(S["Hv_made"], 1)

                    def scale_logits(t):
                        after(dve, S["L_done"], t)
                        nc.vector.tensor_tensor(logit[:, t.slot], bank_rows[:, 0:D], expG[:, t.ring], ALU.mult
                                                ).then_inc(S["logit_made"], 1)
                        after(dve, S["logit_made"], t)
                        nc.vector.tensor_reduce(top[:, t.slot], heads_of(logit[:, t.slot]), AX.X, ALU.max
                                                ).then_inc(S["top_made"], 1)
                        after(dve, S["top_made"], t)
                        after(dve, S["prob_made"], t, lag=2)
                        nc.vector.tensor_tensor(heads_of(centred_logit[:, t.slot]), heads_of(logit[:, t.slot]),
                                                per_head(top[:, t.slot]), ALU.subtract
                                                ).then_inc(S["logit_centred"], 1)

                    def add_Hk(t):
                        if t.chunk == CHUNKS - 1:
                            return
                        after_chunk(dve, S["Hk_update_done"], t, EARLIER)
                        update = pairs_of(bank_sT[:, 0:D])
                        if t.chunk:
                            nc.vector.tensor_tensor(Hk_sum[:, :, :], Hk[:, :, :], update, ALU.add
                                                    ).then_inc(S["Hk_sum_made"], 1)
                        else:
                            nc.vector.tensor_copy(Hk_sum[:, :, :], update).then_inc(S["Hk_sum_made"], 1)

                    def decay_Hk(t):
                        if t.chunk:
                            after_chunk(dve, S["decay_own_made"], t, LATER)
                            after_chunk(dve, S["Hk_sum_made"], t, EARLIER, lag=1)
                            nc.vector.tensor_tensor(Hk[:, :, :], Hk_sum[:, :, :], pairs_of(decay_own[:, t.slot]),
                                                    ALU.mult).then_inc(S["Hk_made"], 1)

                    def totals(t):
                        after(dve, S["prob_made"], t)
                        nc.vector.tensor_reduce(total[:, t.slot], heads_of(prob[:, t.slot]), AX.X, ALU.add
                                                ).then_inc(S["total_made"], 1)
                        after(dve, S["total_made"], t)
                        nc.vector.reciprocal(inv_total[:, t.slot], total[:, t.slot]
                                             ).then_inc(S["inv_total_made"], 1)

                    def o_low(t):
                        after(dve, S["o_high_made"], t)
                        nc.vector.tensor_tensor(o_hl[:, t.slot, 1], o_norm[:, t.slot], o_hl[:, t.slot, 0],
                                                ALU.subtract).then_inc(S["o_low_made"], 1)

                    def make_St(t):
                        after(dve, S["expnG_made"], t)
                        after(dve, S["keep_made"], t)
                        after(dve, S["o_done"], t, lag=4)
                        nc.vector.scalar_tensor_tensor(St[:, t.ring], keep[:, t.slot], 1.0, expnG[:, t.slot],
                                                       ALU.subtract, ALU.mult, reverse0=True
                                                       ).then_inc(S["St_made"], 1)

                    def finish(t):
                        after(dve, S["proj_done"], t)
                        after_dma(dve, res_loaded, t)
                        after_dma(dve, out_stored, t, lag=2)
                        nc.vector.scalar_tensor_tensor(x_out[:, t.slot], bank_qk[:, 0:D], HD ** 0.5 / S_ATT,
                                                       x_res[:, t.slot], ALU.mult, ALU.add
                                                       ).then_inc(S["att_res_added"], 1)

                    pipeline(dve, [(lambda t: norm.stats(dve, t), 3), (gate_abs, 1), (mask_A, 0), (gate_logsig, 1),
                                   (o_low, -2), (qk_abs, 1), (scale_logits, 0),
                                   (lambda t: norm.aggregate(dve, t), 3), (qk_logsig, 1), (mask_B, -1),
                                   (totals, 0), (add_Hv, -1), (add_Hk, 0), (divide_o, -1),
                                   (lambda t: norm.low(dve, t), 3), (make_St, 1), (sum_squares, -1), (finish, -2),
                                   (decay_Hk, 1), (decay_Hv, -1)],
                             tiles, base, UNROLL, LONGEST_LAG)

                @block.tensor
                def _(pe):
                    def project(dst, t, first, last):
                        return three(dst, lambda p, k: xT_hl[:, t.slot, p, k],
                                     lambda p, k: wqkfv_hl[:, p, k, first * D:last * D], KD)

                    def transpose_Pt(t):
                        after(pe, S["Pt_made"], t)
                        after(pe, S["StT_made"], t, lag=-1)
                        for a in range(PAIRS):
                            last = nc.tensor.transpose(bank_sT[:, a * P:(a + 1) * P], Pt[:, t.slot, a * P:(a + 1) * P],
                                                       ident32[:, :])
                        last.then_inc(S["PtT_done"], 1)

                    def project_fv(t):
                        after(pe, norm.xT_made, t)
                        after(pe, S["expG_made"], t, lag=1)
                        after_chunk(pe, S["decay_rows_made"], t, LATER, lag=1)
                        project(bank_fv[:, :], t, 2, 4).then_inc(S["fv_done"], 1)

                    def head_products(t, left, right, done):
                        for z in range(2):
                            rows = slice(z * HD, (z + 1) * HD)
                            for a in range(PAIRS):
                                last = nc.tensor.matmul(bank_pair[:, z * BANK + a * P:z * BANK + (a + 1) * P],
                                                        left(rows, a), right(rows, a), start=True, stop=True)
                        last.then_inc(done, 1)

                    def products_B(t):
                        after(pe, S["PtT_made"], t)
                        after(pe, S["A_made"], t, lag=-1)
                        head_products(t, lambda r, a: StT[r, t.slot, a], lambda r, a: PtT[r, t.slot, a],
                                      S["B_done"])

                    def transpose_qk(t):
                        after(pe, S["qk_made"], t)
                        after_chunk(pe, S["Hv_sum_made"], t, EARLIER, lag=2)
                        for n in range(2):
                            for a in range(PAIRS):
                                at = (n * PAIRS + a) * P
                                last = nc.tensor.transpose(bank_qkT[:, at:at + P],
                                                           qk[:, t.ring, n, a * P:(a + 1) * P], ident32[:, :])
                        last.then_inc(S["qkT_done"], 1)

                    def project_qk(t):
                        after(pe, S["att_res_added"], t, lag=4)
                        project(bank_qk[:, :], t, 0, 2).then_inc(S["qk_done"], 1)

                    def with_state(t, left, state, made, inner, ready, right, done):
                        after_chunk(pe, made, t, LATER)
                        after(pe, ready, t)
                        for a in range(PAIRS):
                            if t.chunk:
                                nc.tensor.matmul(bank_rows[:, a * P:(a + 1) * P], left[:, t.slot, a], state[:, a],
                                                 start=True, stop=True)
                            for z in range(2):
                                at = a * P + z * HD
                                last = nc.tensor.matmul(bank_rows[:, at:at + HD], inner[:, z, a],
                                                        right[:, at:at + HD], start=(t.chunk == 0),
                                                        stop=True,
                                                        skip_group_check=True)
                        last.then_inc(done, 1)

                    def read_out(t):
                        after(pe, S["logit_made"], t, lag=-1)
                        with_state(t, PtT, Hv, S["Hv_made"], B_masked, S["B_made"], qkfv[:, t.ring, 3], S["o_done"])

                    def products_A(t):
                        after(pe, S["qkT_made"], t)
                        after(pe, S["B_made"], t, lag=2)
                        head_products(t, lambda r, a: qkT[r, t.slot, PAIRS + a], lambda r, a: qkT[r, t.slot, a],
                                      S["A_done"])

                    def transpose_St(t):
                        after(pe, S["St_made"], t)
                        after(pe, S["PtT_made"], t, lag=2)
                        after_chunk(pe, S["Hk_sum_made"], t, EARLIER, lag=1)
                        for a in range(PAIRS):
                            last = nc.tensor.transpose(bank_sT[:, a * P:(a + 1) * P],
                                                       St[:, t.ring, a * P:(a + 1) * P], ident32[:, :])
                        last.then_inc(S["StT_done"], 1)

                    def update_Hv(t):
                        if t.chunk < CHUNKS - 1:
                            after(pe, S["qkT_made"], t, lag=-1)
                            for a in range(PAIRS):
                                cols = slice(a * P, (a + 1) * P)
                                last = nc.tensor.matmul(bank_qkT[:, cols], St[:, t.ring, cols],
                                                        qkfv[:, t.ring, 3, cols], start=True, stop=True)
                            last.then_inc(S["Hv_update_done"], 1)

                    def logits(t):
                        after(pe, S["o_raw_made"], t, lag=2)
                        with_state(t, qkT, Hk, S["Hk_made"], A_masked, S["A_made"], St[:, t.ring], S["L_done"])

                    def update_Hk(t):
                        if t.chunk < CHUNKS - 1:
                            after(pe, S["PtT_made"], t, lag=1)
                            after(pe, S["StT_made"], t)
                            for a in range(PAIRS):
                                cols = slice(a * P, (a + 1) * P)
                                last = nc.tensor.matmul(bank_sT[:, cols], qk[:, t.ring, 1, cols], St[:, t.ring, cols],
                                                        start=True, stop=True)
                            last.then_inc(S["Hk_update_done"], 1)

                    def transpose_o(t):
                        after(pe, S["o_low_made"], t)
                        after(pe, norm.xT_made, t, lag=-3)
                        for part in range(2):
                            for k in range(KD):
                                at = (part * KD + k) * P
                                last = nc.tensor.transpose(xT_ps[:, at:at + P], o_hl[:, t.slot, part, k * P:(k + 1) * P],
                                                           ident16[:, :])
                        last.then_inc(S["oT_done"], 1)

                    def log_gate_sums(t):
                        after(pe, S["gate_low"], t)
                        now = gate_hl[:, t.slot]
                        before = gate_hl[:, 1 - t.slot]
                        for part in range(2):
                            last = nc.tensor.matmul(bank_fv[:, 0:D], ramp16[:, :], now[:, part],
                                                    start=(part == 0), stop=(part == 1))
                        if t.chunk:
                            terms = [(late16, before), (early16, now)]
                            for n, (ones, gates) in enumerate(terms):
                                for part in range(2):
                                    last = nc.tensor.matmul(bank_fv[:, D:2 * D], ones[:, :], gates[:, part],
                                                            start=(n == 0 and part == 0), stop=(n == 1 and part == 1))
                        last.then_inc(S["G_done"], 1)
                        if t.chunk:
                            after(pe, S["oT_made"], t, lag=3)
                            after(pe, norm.xT_made, t)
                            for a in range(PAIRS):
                                for n, (ones, gates) in enumerate(terms):
                                    for part in range(2):
                                        last = nc.tensor.matmul(bank_16[:, a:a + 1],
                                                                gates[:, part, a * P:(a + 1) * P], ones[:, 0:1],
                                                                start=(n == 0 and part == 0),
                                                                stop=(n == 1 and part == 1))
                            last.then_inc(S["decay_col_done"], 1)

                    def project_out(t):
                        after(pe, S["oT_made"], t)
                        after(pe, S["qk_raw_made"], t, lag=-3)
                        three(bank_qk[:, 0:D], lambda p, k: oT[:, t.slot, p, k], lambda p, k: wo_hl[:, p, k],
                              KD).then_inc(S["proj_done"], 1)

                    def transpose_x(t):
                        after_chunk(pe, S["decay_col_made"], t, LATER, lag=1)
                        after(pe, S["oT_made"], t, lag=4)
                        norm.transpose(pe, t, xT_ps)

                    pipeline(pe, [(transpose_qk, 0), (project_fv, 1), (products_A, 0), (project_qk, 1),
                                  (transpose_St, 0), (logits, 0), (transpose_o, -2), (transpose_Pt, -1),
                                  (update_Hv, -1), (log_gate_sums, 1), (products_B, -1), (update_Hk, 0),
                                  (transpose_x, 2), (project_out, -2), (read_out, -1)],
                             tiles, base, UNROLL, LONGEST_LAG)
            scope.close()

        norm = Norm("ffn")
        res_loaded, out_stored = pair("res_loaded"), pair("out_stored")
        low_done, low_high_made = sem("low_done"), sem("low_high_made")
        low_h1_made, low_low_made = sem("low_h1_made"), sem("low_low_made")
        logits_done, runmax_made, step_made = sem("logits_done"), sem("runmax_made"), sem("step_made")
        onehot_made, mid_done = sem("onehot_made"), sem("mid_done")
        mid_high_made, mid_low_made, masked = sem("mid_high_made"), sem("mid_low_made"), sem("masked")
        hotT_done, hotT_made = sem("hotT_done"), sem("hotT_made")
        res_done, res_biased, out_made = sem("res_done"), sem("res_biased"), sem("out_made")

        x1 = nc.dram_tensor("x1", [tiles * P, d_model], f32, kind="Internal").ap()
        x2 = nc.dram_tensor("x2", [tiles * P, d_model], f32, kind="Internal").ap()
        ffn_phase(a["x"], x1, 0)
        attention_phase(x1, x2)
        ffn_phase(x2, out, tiles)


INPUTS = {
    "x": "L0_attn_x", "Wq": "L0_attn_Wq", "Wk": "L0_attn_Wk", "Wv": "L0_attn_Wv", "Wf": "L0_attn_Wf",
    "g": "L0_attn_g_norm_w", "Wo": "L0_attn_Wo", "m1": "L0_ffn_m1", "m2": "L0_ffn_m2", "mb": "L0_ffn_mb",
    "w1": "L0_ffn_w1", "w2": "L0_ffn_w2", "b2": "L0_ffn_b2",
}


def kernel(**inputs):
    import numpy as _np
    import concourse.bacc as _bacc
    from concourse import mybir as _mybir
    from concourse.bass_utils import run_bass_kernel_spmd as _run

    nc = _bacc.Bacc("TRN2", target_bir_lowering=False, num_devices=1)
    arrays, a = {}, {}
    for short, name in INPUTS.items():
        arr = _np.ascontiguousarray(inputs[name])
        if short == "x":
            shape = arr.shape
            arr = arr.reshape(-1, shape[-1])
        arrays[f"in_{name}"] = arr
        a[short] = nc.dram_tensor(f"in_{name}", arr.shape, _mybir.dt.from_np(arr.dtype), kind="ExternalInput").ap()
    tokens, d_model = arrays["in_L0_attn_x"].shape
    d_low, groups, d2 = arrays["in_L0_ffn_m2"].shape
    heads = d_model // arrays["in_L0_attn_g_norm_w"].shape[0]
    out = nc.dram_tensor("out", (tokens, d_model), _mybir.dt.float32, kind="ExternalOutput").ap()
    build(nc, a, out, tokens // P, d_model, groups * d2, d2, d_low, heads)
    r = _run(nc, [arrays], core_ids=[0])
    return r.results[0]["out"].reshape(shape)
```
